# Optimizing a Trainium2 kernel written in Bass

```python
import numpy as np
import jax
import jax.numpy as jnp

def _softmax(x, axis=-1):
    return jax.nn.softmax(x, axis=axis)

def _gelu(x):
    return jax.nn.gelu(x, approximate=True)

def _silu(x):
    return jax.nn.silu(x)

def _sigmoid(x):
    return jax.nn.sigmoid(x)

def _layernorm(x, axis=-1, eps=1e-05):
    m = jnp.mean(x, axis=axis, keepdims=True)
    v = jnp.var(x, axis=axis, keepdims=True)
    return (x - m) / jnp.sqrt(v + eps)

def _scatter_add(tgt, idx, src, axis=0):
    return tgt.at[idx].add(src)

def _segment_sum(src, seg, n):
    return jax.ops.segment_sum(src, seg, n)
kernel_name = 'mk_macaron_d2_jaxref_r8_fbbd60'

def setup_inputs(seed: int=0):
    np.random.seed(seed)
    _w = jnp.asarray

    def _L0_attn_setup():
        import jax, jax.numpy as jnp
        import numpy as np
        HIDDEN = 128
        NUM_HEADS = 16
        NUM_KV = 4
        HEAD_DIM = HIDDEN // NUM_HEADS
        GROUPS = NUM_HEADS // NUM_KV
        SCALE = HEAD_DIM ** 0.5
        key = jax.random.key(seed)
        ks = jax.random.split(key, 9)
        s = 0.02
        B, N = (4, 256)
        return {'x': jax.random.normal(ks[0], (B, N, HIDDEN), dtype=jnp.float32), 'Wq': jax.random.normal(ks[1], (HIDDEN, NUM_HEADS * HEAD_DIM), dtype=jnp.float32) * s, 'bq': jnp.zeros((NUM_HEADS * HEAD_DIM,), dtype=jnp.float32), 'Wk': jax.random.normal(ks[2], (HIDDEN, NUM_KV * HEAD_DIM), dtype=jnp.float32) * s, 'bk': jnp.zeros((NUM_KV * HEAD_DIM,), dtype=jnp.float32), 'Wv': jax.random.normal(ks[3], (HIDDEN, NUM_KV * HEAD_DIM), dtype=jnp.float32) * s, 'bv': jnp.zeros((NUM_KV * HEAD_DIM,), dtype=jnp.float32), 'Wo': jax.random.normal(ks[4], (NUM_HEADS * HEAD_DIM, HIDDEN), dtype=jnp.float32) * s, 'bo': jnp.zeros((HIDDEN,), dtype=jnp.float32)}
    _L0_attn_in = _L0_attn_setup()

    def _L0_ffn_setup():
        import jax, jax.numpy as jnp
        import numpy as np
        HIDDEN_SIZE = 128
        NUM_EXPERTS = 8
        MOE_INTERMEDIATE_SIZE = 176
        NUM_EXPERTS_PER_TOK = 2
        SHARED_EXPERT_INTERMEDIATE_SIZE = 352
        B, T = (2, 128)
        W_SCALE = 0.02
        key = jax.random.key(seed)
        ks = jax.random.split(key, 8)
        H, E, I, SI = (HIDDEN_SIZE, NUM_EXPERTS, MOE_INTERMEDIATE_SIZE, SHARED_EXPERT_INTERMEDIATE_SIZE)
        return {'x': jax.random.normal(ks[0], (B, T, H), jnp.float32), 'gate_w': jax.random.normal(ks[1], (E, H), jnp.float32) * W_SCALE, 'experts_gate_up': jax.random.normal(ks[2], (E, 2 * I, H), jnp.float32) * W_SCALE, 'experts_down': jax.random.normal(ks[3], (E, H, I), jnp.float32) * W_SCALE, 'shared_gate_w': jax.random.normal(ks[4], (SI, H), jnp.float32) * W_SCALE, 'shared_up_w': jax.random.normal(ks[5], (SI, H), jnp.float32) * W_SCALE, 'shared_down_w': jax.random.normal(ks[6], (H, SI), jnp.float32) * W_SCALE, 'shared_expert_gate_w': jax.random.normal(ks[7], (1, H), jnp.float32) * W_SCALE}
    _L0_ffn_in = _L0_ffn_setup()

    def _L1_attn_setup():
        import jax, jax.numpy as jnp
        import numpy as np
        import math
        D_MODEL, N_HEADS, D_K, D_C, D_HR = (128, 8, 128, 32, 32)
        B, S = (4, 256)
        key = jax.random.key(seed)
        ks = jax.random.split(key, 17)

        def lin(k, fan_in, fan_out):
            lim = 1.0 / math.sqrt(fan_in)
            kw, kb = jax.random.split(k)
            W = jax.random.uniform(kw, (fan_in, fan_out), jnp.float32, -lim, lim)
            b = jax.random.uniform(kb, (fan_out,), jnp.float32, -lim, lim)
            return (W, b)
        W_DQ, b_DQ = lin(ks[0], D_MODEL, D_C)
        W_UQ, b_UQ = lin(ks[1], D_C, N_HEADS * D_K)
        W_DKV, b_DKV = lin(ks[2], D_MODEL, D_C)
        W_UK, b_UK = lin(ks[3], D_C, N_HEADS * D_K)
        W_UV, b_UV = lin(ks[4], D_C, N_HEADS * D_K)
        W_QR, b_QR = lin(ks[5], D_C, N_HEADS * D_HR)
        W_KR, b_KR = lin(ks[6], D_MODEL, D_HR)
        W_O, b_O = lin(ks[7], N_HEADS * D_K, D_MODEL)
        h_t = jax.random.normal(ks[8], (B, S, D_MODEL), jnp.float32)
        return {'h_t': h_t, 'W_DQ': W_DQ, 'b_DQ': b_DQ, 'W_UQ': W_UQ, 'b_UQ': b_UQ, 'W_DKV': W_DKV, 'b_DKV': b_DKV, 'W_UK': W_UK, 'b_UK': b_UK, 'W_UV': W_UV, 'b_UV': b_UV, 'W_QR': W_QR, 'b_QR': b_QR, 'W_KR': W_KR, 'b_KR': b_KR, 'W_O': W_O, 'b_O': b_O}
    _L1_attn_in = _L1_attn_setup()

    def _L1_ffn_setup():
        import jax, jax.numpy as jnp
        import numpy as np
        D_MODEL = 128
        D_FF = 512
        N_ZONES = 8
        TOP_K = 3
        ROUTER_H = 32
        BATCH = 16
        SEQ = 256
        key = jax.random.key(seed)
        ks = jax.random.split(key, 8)
        s = lambda *dims: 1.0 / np.sqrt(dims[-2] if len(dims) > 1 else dims[-1])
        x = jax.random.normal(ks[0], (BATCH, SEQ, D_MODEL), dtype=jnp.float32)
        W1 = jax.random.normal(ks[1], (D_MODEL, ROUTER_H), dtype=jnp.float32) / np.sqrt(D_MODEL)
        b1 = jnp.zeros((ROUTER_H,), dtype=jnp.float32)
        W2 = jax.random.normal(ks[2], (ROUTER_H, N_ZONES), dtype=jnp.float32) / np.sqrt(ROUTER_H)
        b2 = jnp.zeros((N_ZONES,), dtype=jnp.float32)
        Wa = jax.random.normal(ks[3], (N_ZONES, D_MODEL, D_FF), dtype=jnp.float32) / np.sqrt(D_MODEL)
        Wb = jax.random.normal(ks[4], (N_ZONES, D_FF, D_MODEL), dtype=jnp.float32) / np.sqrt(D_FF)
        return {'x': x, 'W1': W1, 'b1': b1, 'W2': W2, 'b2': b2, 'Wa': Wa, 'Wb': Wb}
    _L1_ffn_in = _L1_ffn_setup()
    _d = {'L0_attn_x': _L0_attn_in['x'], 'L0_attn_Wq': _L0_attn_in['Wq'], 'L0_attn_bq': _L0_attn_in['bq'], 'L0_attn_Wk': _L0_attn_in['Wk'], 'L0_attn_bk': _L0_attn_in['bk'], 'L0_attn_Wv': _L0_attn_in['Wv'], 'L0_attn_bv': _L0_attn_in['bv'], 'L0_attn_Wo': _L0_attn_in['Wo'], 'L0_attn_bo': _L0_attn_in['bo'], 'L0_ffn_gate_w': _L0_ffn_in['gate_w'], 'L0_ffn_experts_gate_up': _L0_ffn_in['experts_gate_up'], 'L0_ffn_experts_down': _L0_ffn_in['experts_down'], 'L0_ffn_shared_gate_w': _L0_ffn_in['shared_gate_w'], 'L0_ffn_shared_up_w': _L0_ffn_in['shared_up_w'], 'L0_ffn_shared_down_w': _L0_ffn_in['shared_down_w'], 'L0_ffn_shared_expert_gate_w': _L0_ffn_in['shared_expert_gate_w'], 'L1_attn_W_DQ': _L1_attn_in['W_DQ'], 'L1_attn_b_DQ': _L1_attn_in['b_DQ'], 'L1_attn_W_UQ': _L1_attn_in['W_UQ'], 'L1_attn_b_UQ': _L1_attn_in['b_UQ'], 'L1_attn_W_DKV': _L1_attn_in['W_DKV'], 'L1_attn_b_DKV': _L1_attn_in['b_DKV'], 'L1_attn_W_UK': _L1_attn_in['W_UK'], 'L1_attn_b_UK': _L1_attn_in['b_UK'], 'L1_attn_W_UV': _L1_attn_in['W_UV'], 'L1_attn_b_UV': _L1_attn_in['b_UV'], 'L1_attn_W_QR': _L1_attn_in['W_QR'], 'L1_attn_b_QR': _L1_attn_in['b_QR'], 'L1_attn_W_KR': _L1_attn_in['W_KR'], 'L1_attn_b_KR': _L1_attn_in['b_KR'], 'L1_attn_W_O': _L1_attn_in['W_O'], 'L1_attn_b_O': _L1_attn_in['b_O'], 'L1_ffn_W1': _L1_ffn_in['W1'], 'L1_ffn_b1': _L1_ffn_in['b1'], 'L1_ffn_W2': _L1_ffn_in['W2'], 'L1_ffn_b2': _L1_ffn_in['b2'], 'L1_ffn_Wa': _L1_ffn_in['Wa'], 'L1_ffn_Wb': _L1_ffn_in['Wb']}
    _x0 = _d['L0_attn_x']
    _d['L0_attn_x'] = jax.random.normal(jax.random.fold_in(jax.random.key(seed), 1), (16, 256, 128), dtype=_x0.dtype)
    del _x0
    return _d

def reference(L0_attn_x, L0_attn_Wq, L0_attn_bq, L0_attn_Wk, L0_attn_bk, L0_attn_Wv, L0_attn_bv, L0_attn_Wo, L0_attn_bo, L0_ffn_gate_w, L0_ffn_experts_gate_up, L0_ffn_experts_down, L0_ffn_shared_gate_w, L0_ffn_shared_up_w, L0_ffn_shared_down_w, L0_ffn_shared_expert_gate_w, L1_attn_W_DQ, L1_attn_b_DQ, L1_attn_W_UQ, L1_attn_b_UQ, L1_attn_W_DKV, L1_attn_b_DKV, L1_attn_W_UK, L1_attn_b_UK, L1_attn_W_UV, L1_attn_b_UV, L1_attn_W_QR, L1_attn_b_QR, L1_attn_W_KR, L1_attn_b_KR, L1_attn_W_O, L1_attn_b_O, L1_ffn_W1, L1_ffn_b1, L1_ffn_W2, L1_ffn_b2, L1_ffn_Wa, L1_ffn_Wb):

    def _L0_attn_ref(x, Wq, bq, Wk, bk, Wv, bv, Wo, bo):
        import jax, jax.numpy as jnp
        import numpy as np
        HIDDEN = 128
        NUM_HEADS = 16
        NUM_KV = 4
        HEAD_DIM = HIDDEN // NUM_HEADS
        GROUPS = NUM_HEADS // NUM_KV
        SCALE = HEAD_DIM ** 0.5
        B, N, _ = x.shape
        q = x @ Wq + bq
        k = x @ Wk + bk
        v = x @ Wv + bv
        q = q.reshape(B, N, NUM_HEADS, HEAD_DIM).transpose(0, 2, 1, 3)
        q = q.reshape(B, NUM_KV, GROUPS, N, HEAD_DIM).transpose(0, 2, 1, 3, 4)
        k = k.reshape(B, N, NUM_KV, HEAD_DIM).transpose(0, 2, 1, 3)
        v = v.reshape(B, N, NUM_KV, HEAD_DIM).transpose(0, 2, 1, 3)
        scores = jnp.einsum('bghnd,bhsd->bghns', q, k)
        attn = jax.nn.softmax(scores / SCALE, axis=-1)
        out = jnp.einsum('bghns,bhsd->bghnd', attn, v)
        out = out.transpose(0, 3, 1, 2, 4).reshape(B, N, NUM_HEADS * HEAD_DIM)
        return out @ Wo + bo

    def _L0_ffn_ref(x, gate_w, experts_gate_up, experts_down, shared_gate_w, shared_up_w, shared_down_w, shared_expert_gate_w):
        import jax, jax.numpy as jnp
        import numpy as np
        HIDDEN_SIZE = 128
        NUM_EXPERTS = 8
        MOE_INTERMEDIATE_SIZE = 176
        NUM_EXPERTS_PER_TOK = 2
        SHARED_EXPERT_INTERMEDIATE_SIZE = 352
        B, T = (2, 128)
        W_SCALE = 0.02
        Bx, Tx, H = x.shape
        E = gate_w.shape[0]
        I = experts_down.shape[2]
        x_flat = x.reshape(Bx * Tx, H)
        logits = x_flat @ gate_w.T
        scores = jax.nn.softmax(logits, axis=-1)
        _, topk_ids = jax.lax.top_k(scores, NUM_EXPERTS_PER_TOK)
        in_topk = jax.nn.one_hot(topk_ids, E, dtype=x.dtype).sum(axis=1)
        w = scores * in_topk
        gu = jnp.einsum('nh,eih->nei', x_flat, experts_gate_up)
        g, u = (gu[..., :I], gu[..., I:])
        h = jax.nn.silu(g) * u
        expert_out = jnp.einsum('nei,ehi->neh', h, experts_down)
        out = jnp.einsum('neh,ne->nh', expert_out, w)
        shared = jax.nn.silu(x_flat @ shared_gate_w.T) * (x_flat @ shared_up_w.T) @ shared_down_w.T
        shared_weight = jax.nn.sigmoid(x_flat @ shared_expert_gate_w.T)
        out = out + shared_weight * shared
        return out.reshape(Bx, Tx, H)

    def _L1_attn_ref(h_t, W_DQ, b_DQ, W_UQ, b_UQ, W_DKV, b_DKV, W_UK, b_UK, W_UV, b_UV, W_QR, b_QR, W_KR, b_KR, W_O, b_O):
        import jax, jax.numpy as jnp
        import numpy as np
        import math
        D_MODEL, N_HEADS, D_K, D_C, D_HR = (128, 8, 128, 32, 32)
        B, S = (4, 256)
        b, s, _ = h_t.shape
        c_q = h_t @ W_DQ + b_DQ
        c_kv = h_t @ W_DKV + b_DKV
        q_c = (c_q @ W_UQ + b_UQ).reshape(b, s, N_HEADS, D_K).transpose(0, 2, 1, 3)
        k_c = (c_kv @ W_UK + b_UK).reshape(b, s, N_HEADS, D_K).transpose(0, 2, 1, 3)
        v_c = (c_kv @ W_UV + b_UV).reshape(b, s, N_HEADS, D_K).transpose(0, 2, 1, 3)
        q_r = (c_q @ W_QR + b_QR).reshape(b, s, N_HEADS, D_HR).transpose(0, 2, 1, 3)
        k_r = (h_t @ W_KR + b_KR)[:, None, :, :]
        k_r = jnp.broadcast_to(k_r, (b, N_HEADS, s, D_HR))
        q = jnp.concatenate([q_c, q_r], axis=-1)
        k = jnp.concatenate([k_c, k_r], axis=-1)
        scale = 1.0 / math.sqrt(D_K + D_HR)
        scores = jnp.einsum('bhsd,bhtd->bhst', q, k) * scale
        attn = jax.nn.softmax(scores, axis=-1)
        o = jnp.einsum('bhst,bhtd->bhsd', attn, v_c)
        o = o.transpose(0, 2, 1, 3).reshape(b, s, N_HEADS * D_K)
        return o @ W_O + b_O

    def _L1_ffn_ref(x, W1, b1, W2, b2, Wa, Wb):
        import jax, jax.numpy as jnp
        import numpy as np
        D_MODEL = 128
        D_FF = 512
        N_ZONES = 8
        TOP_K = 3
        ROUTER_H = 32
        BATCH = 16
        SEQ = 256
        pooled = x.mean(axis=1)
        h = jnp.tanh(pooled @ W1 + b1)
        logits = h @ W2 + b2
        probs = jax.nn.softmax(logits, axis=-1)
        top_p, top_i = jax.lax.top_k(probs, TOP_K)
        top_w = top_p / top_p.sum(axis=-1, keepdims=True)
        onehot = jax.nn.one_hot(top_i, N_ZONES, dtype=x.dtype)
        w = jnp.einsum('bk,bke->be', top_w, onehot)
        zone_outputs = jnp.zeros_like(x)
        for e in range(N_ZONES):
            z = jax.nn.gelu(x @ Wa[e]) @ Wb[e]
            zone_outputs = zone_outputs + z * w[:, e, None, None]
        return x + zone_outputs
    x = L0_attn_x
    x = x + 0.5 * _L0_ffn_ref(_layernorm(x, axis=-1), L0_ffn_gate_w, L0_ffn_experts_gate_up, L0_ffn_experts_down, L0_ffn_shared_gate_w, L0_ffn_shared_up_w, L0_ffn_shared_down_w, L0_ffn_shared_expert_gate_w)
    x = x + _L0_attn_ref(_layernorm(x, axis=-1), L0_attn_Wq, L0_attn_bq, L0_attn_Wk, L0_attn_bk, L0_attn_Wv, L0_attn_bv, L0_attn_Wo, L0_attn_bo)
    x = x + 0.5 * _L0_ffn_ref(_layernorm(x, axis=-1), L0_ffn_gate_w, L0_ffn_experts_gate_up, L0_ffn_experts_down, L0_ffn_shared_gate_w, L0_ffn_shared_up_w, L0_ffn_shared_down_w, L0_ffn_shared_expert_gate_w)
    x = x + 0.5 * _L1_ffn_ref(_layernorm(x, axis=-1), L1_ffn_W1, L1_ffn_b1, L1_ffn_W2, L1_ffn_b2, L1_ffn_Wa, L1_ffn_Wb)
    x = x + _L1_attn_ref(_layernorm(x, axis=-1), L1_attn_W_DQ, L1_attn_b_DQ, L1_attn_W_UQ, L1_attn_b_UQ, L1_attn_W_DKV, L1_attn_b_DKV, L1_attn_W_UK, L1_attn_b_UK, L1_attn_W_UV, L1_attn_b_UV, L1_attn_W_QR, L1_attn_b_QR, L1_attn_W_KR, L1_attn_b_KR, L1_attn_W_O, L1_attn_b_O)
    x = x + 0.5 * _L1_ffn_ref(_layernorm(x, axis=-1), L1_ffn_W1, L1_ffn_b1, L1_ffn_W2, L1_ffn_b2, L1_ffn_Wa, L1_ffn_Wb)
    return x

_drawn_inputs = setup_inputs


def setup_inputs(seed=0):
    import zlib

    import numpy as np

    out = dict(_drawn_inputs(seed))
    spreads = {'L0_attn_bq': (0.0, 0.8),
     'L0_attn_bk': (0.0, 2.0),
     'L0_attn_bv': (0.0, 0.1),
     'L0_attn_bo': (0.0, 0.1),
     'L1_ffn_b1': (0.0, 0.1),
     'L1_ffn_b2': (0.0, 0.1)}
    factors = {'L0_attn_Wq': 8.0,
     'L0_attn_Wk': 8.0,
     'L0_attn_Wv': 8.0,
     'L0_ffn_gate_w': 8.0,
     'L0_ffn_experts_gate_up': 8.0,
     'L0_ffn_experts_down': 8.0,
     'L0_ffn_shared_gate_w': 8.0,
     'L0_ffn_shared_up_w': 8.0,
     'L0_ffn_shared_down_w': 8.0,
     'L0_ffn_shared_expert_gate_w': 8.0,
     'L1_attn_W_DQ': 8.0,
     'L1_attn_b_DQ': 8.0,
     'L1_attn_W_UQ': 8.0,
     'L1_attn_b_UQ': 8.0,
     'L1_attn_b_DKV': 6.434,
     'L1_attn_W_UK': 8.0,
     'L1_attn_b_UK': 64.0,
     'L1_attn_W_UV': 2.671,
     'L1_attn_W_QR': 8.0,
     'L1_attn_b_QR': 24.435,
     'L1_attn_W_KR': 8.0,
     'L1_attn_b_KR': 64.0,
     'L1_attn_b_O': 4.487,
     'L1_attn_b_UV': 3.673}
    for name, (base, spread) in spreads.items():
        noise = np.random.default_rng([zlib.crc32(name.encode()), seed]).standard_normal(out[name].shape)
        drawn = base * np.exp(spread * noise) if base else spread * noise
        out[name] = jnp.asarray(drawn.astype(out[name].dtype))
    for name, factor in factors.items():
        out[name] = (out[name] * factor).astype(out[name].dtype)
    return out
```

```python
from collections import namedtuple
from contextlib import ExitStack

import numpy as np

import concourse.bass as bass
from concourse import mybir

F32 = mybir.dt.float32
F32R = mybir.dt.float32r
I32 = mybir.dt.int32
ALU = mybir.AluOpType
ACT = mybir.ActivationFunctionType
AX = mybir.AxisListType

P = 128
H = 128
NB, SEQ = 16, 256
NT = NB * SEQ // P
TPB = SEQ // P
TPC = 4
NC = NT // TPC
EPS = 1e-5
E0, I0, SI0, TOP0 = 8, 176, 352, 2
MT0 = -(-(E0 * I0 + SI0) // P)
NG0 = E0 + 1
GC = NG0 + 1
NH0, NKV0, HD0 = 16, 4, 8
GQ0 = NH0 // NKV0
SC0 = float(HD0) ** -0.5
NH1, DK1, DC1, DR1 = 8, 128, 32, 32
KAP = DC1 + DR1 + 1
SC1 = float(DK1 + DR1) ** -0.5
E1, FF1, RH1, TOP1 = 8, 512, 32, 3
FT1 = FF1 // P


def names(items):
    return namedtuple("Names", items)(**items)


class Buffers:
    pass


def wait(eng, sem, value, start=0):
    if not (isinstance(value, int) and value <= 0):
        eng.wait_ge(sem, start + value)


def by_parity(eng, step):
    step(0, 0)
    step(1, 1)
    with eng.Fori(1, NC // 2) as i:
        step(2 * i, 0)
        step(2 * i + 1, 1)


class Chain:

    def __init__(self, eng, sem, start=0):
        self.eng, self.sem, self.start, self.base, self.n = eng, sem, start, 0, 0

    def link(self, ins):
        self.n += 1
        ins.then_inc(self.sem, 1)
        self.eng.wait_ge(self.sem, self.start + self.base + self.n)


SMALL = dict(wqs=GQ0 * P, wks=P, wv=NKV0 * HD0, bqk=GQ0 + 1, bvb=NKV0 * HD0, wo=H, bo=H, masks=8, w1=RH1, b1=1, w2=E1, b2=E1,
             diag=NB, rev=E1, wdqs=P, wkap=DC1 + DR1, wckv=DC1, b1q=1, b1k=1, bckv=DC1, bo1=H, gw=GC, eps=1, ident=P, ones=P,
             pool=NB)
SMALL_N = sum(SMALL.values())
RAW1_PARTS = dict(ukt=NH1 * KAP, uqt=NH1 * P, qrp=NH1 * KAP, spread=P, uvt=NH1 * P, wo=NH1 * H, buv=NH1, neg=NH1 * P)
RAW1_N = sum(RAW1_PARTS.values())


def program(nc, a, out, stages):
    ctx = ExitStack()
    with ctx:
        def sb(name, shape, dt=F32):
            return ctx.enter_context(nc.sbuf_tensor(name, shape, dt))

        def sems(prefix, which):
            return names({n: ctx.enter_context(nc.semaphore(f"{prefix}_{n}")) for n in which.split()})

        PS = ctx.enter_context(nc.psum_tensor("PS", [P, 8, 512], F32))

        def bank(k, n=1):
            return PS[:, k:k + n, :].rearrange("p b n -> p (b n)")

        X = sb("X", [P, NT, H])
        XT = sb("XT", [P, NT * P])
        XHI = sb("XHI", [P, NT * P], F32R)
        XLO = sb("XLO", [P, NT * P], F32R)
        XN = sb("XN", [P, 2, TPC, H])
        STAT = sb("STAT", [P, NT, 6])
        LN = sb("LN", [P, 6, NT])
        RSTD, NBIAS = LN[:, 4, :], LN[:, 5, :]
        WG = [sb(f"WG{i}", [P, MT0 * P], F32R) for i in range(2)]
        WU = [sb(f"WU{i}", [P, MT0 * P], F32R) for i in range(2)]
        WD = [sb(f"WD{i}", [P, MT0, H], F32R) for i in range(2)]
        SEL = sb("SEL", [P, MT0 * P], F32R)
        WTS = sb("WTS", [P, NT * P], F32R)
        AR = sb("AR", [P, 7936])
        RR = sb("RR", [P, 2048], F32R)
        SM = sb("SM", [P, 4352])
        IDX = sb("IDX", [P, NB * TOP1], I32)

        sm_at = [0]

        def small(n):
            sm_at[0] += n
            assert sm_at[0] <= 4352
            return SM[:, sm_at[0] - n:sm_at[0]]

        G = sems("all", "x_in small_in raw_in split stats_new zeroed out_done")

        T = {}
        for name, n in SMALL.items():
            T[name] = small(n)
        T = names(T)
        wstage = small(2 * TPC * NG0)
        VA = small(512).rearrange("p (u k g d) -> p u k g d", u=2, k=2, g=4)
        XTB = small(512).rearrange("p (u n) -> p u n", u=2)
        bs1 = small(NH1 * P)
        cg = small(2 * H)
        cb = small(H)
        rev, ident, ones = T.rev, T.ident, T.ones

        block = ctx.enter_context(nc.Block())

        FFN0 = "stats_done dve_chain gate_chain rstd_in xn tr xt xhi xlo lg_pe lg_dve p_max p_exp w_all ws wt_pe wt_hi wt_lo g_pe u_pe w_pe silu prod gated h_hi h_lo down acc_copied back x_new st_new"
        FFN1 = ("stats_done dve_chain rt_chain sub rstd_in xn tr xt w_in0 w_in1 w_in2 r_pe r_act r_dve idx gelu u_pe z_pe acc_chain sum "
                "back x_half x_new st_new")
        BOTH = ("stats_done dve_chain m_chain r_chain rstd_in xn tr xt xtb kv qh qs kx v s_pe smax mm mt st_pe "
                "exp av os ot ao aot_pe aot out x_new st_new zero")
        kinds = {"f0": FFN0, "f1": FFN1, "a0": BOTH + " k_chain q qx ksz qs2",
                 "a1": BOTH + " kp_pe kp_hi kp_lo mtc raw_in prep_pe prep_copy negsel"}
        SEMS = {kind: sems(kind, which) for kind, which in kinds.items() if kind in stages}
        ST = [SEMS[kind] for kind in stages]
        tiles0, runs = MT0 * NC, {"f0": NC, "f1": NB, "a0": NB, "a1": NB}
        TOTAL = {
            "f0": dict({x: NC for x in "xn tr xt xhi xlo lg_pe lg_dve ws wt_pe wt_hi wt_lo acc_copied back x_new st_new".split()},
                       **{x: tiles0 for x in "g_pe u_pe w_pe silu prod gated h_hi h_lo down".split()},
                       stats_done=1, rstd_in=1, p_max=1, p_exp=2),
            "f1": dict({x: NC for x in "xn tr xt".split()}, **{x: NB for x in "sum back x_half x_new st_new".split()},
                       gelu=6 * NB, u_pe=6 * NB, z_pe=3 * NB, acc_chain=2 * NB, w_in0=32 * NB, w_in1=32 * NB, w_in2=32 * NB,
                       stats_done=1, rstd_in=1, sub=1, r_pe=3, r_act=2, r_dve=1, idx=1),
            "a0": {}, "a1": {}}
        links = {}

        def counts(n):
            kind = stages[n]
            again = stages[:n].count(kind)
            assert not again or kind in ("f0", "f1")
            total = dict(TOTAL[kind])
            for x in kinds[kind].split():
                if x not in total and again:
                    total[x] = links.get((kind, x), 0)
            return names({x: again * total.get(x, 0) for x in kinds[kind].split()})



        def x_done(n):
            if n == 0:
                return G.stats_new, NC
            return ST[n - 1].st_new, counts(n - 1).st_new + runs[stages[n - 1]]

        def norm_dve(n, hilo):
            S, D = ST[n], counts(n)
            v = nc.vector
            sem, count = x_done(n)
            v.wait_ge(sem, count)
            ch = Chain(v, S.dve_chain, D.dve_chain)
            me, mo, ve, vo = STAT[:, :, 1], STAT[:, :, 4], STAT[:, :, 2], STAT[:, :, 5]
            ch.link(v.tensor_tensor(LN[:, 0, :], me, mo, ALU.add))
            ch.link(v.tensor_tensor(LN[:, 1, :], me, mo, ALU.subtract))
            ch.link(v.scalar_tensor_tensor(LN[:, 1, :], LN[:, 1, :], H / 4.0, LN[:, 1, :], ALU.mult, ALU.mult))
            ch.link(v.tensor_tensor(LN[:, 2, :], ve, vo, ALU.add))
            v.tensor_tensor(LN[:, 2, :], LN[:, 1, :], LN[:, 2, :], ALU.add).then_inc(S.stats_done, 1)
            v.wait_ge(S.rstd_in, D.rstd_in + 1)
            ch.link(v.reciprocal(RSTD, LN[:, 3, :]))
            ch.link(v.scalar_tensor_tensor(NBIAS, LN[:, 0, :], -0.5, RSTD, ALU.mult, ALU.mult))
            links[(stages[n], "dve_chain")] = ch.n

            def chunk_step(c, u):
                wait(v, S.tr, c - 1, D.tr)
                for t in range(TPC):
                    k = c * TPC + t
                    last = v.tensor_scalar(XN[:, u, t:t + 1, :], X[:, bass.ds(k, 1), :], RSTD[:, bass.ds(k, 1)],
                                           NBIAS[:, bass.ds(k, 1)], ALU.mult, ALU.add)
                last.then_inc(S.xn, 1)
                if hilo:
                    v.wait_ge(S.xhi, D.xhi + c + 1)
                    v.tensor_tensor(XLO[:, bass.ds(c * 512, 512)], bank(u), XHI[:, bass.ds(c * 512, 512)].bitcast(F32),
                                    ALU.subtract).then_inc(S.xlo, 1)
                    v.wait_ge(S.lg_pe, D.lg_pe + c + 1)
                    v.tensor_copy(LG[:, bass.ds(c * TPC, TPC), :],
                                  bank(2 + u)[:, 0:TPC * GC].rearrange("p (t e) -> p t e", t=TPC)).then_inc(S.lg_dve, 1)

            by_parity(v, chunk_step)

        def norm_pe(n, hilo):
            S, D = ST[n], counts(n)
            pe = nc.tensor

            def chunk_step(c, u):
                pe.wait_ge(S.xn, D.xn + c + 1)
                wait(pe, S.xlo if hilo else S.xt, c - 1, D.xlo if hilo else D.xt)
                for t in range(TPC):
                    last = pe.transpose(bank(u)[:, t * P:(t + 1) * P], XN[:, u, t, :], ident)
                last.then_inc(S.tr, 1)
                if hilo:
                    pe.wait_ge(S.xt, D.xt + c + 1)
                    wait(pe, S.lg_dve, c - 1, D.lg_dve)
                    for t in range(TPC):
                        last = pe.matmul(bank(2 + u)[:, t * GC:(t + 1) * GC], XTC[:, u, t * P:(t + 1) * P], T.gw,
                                         start=True, stop=True)
                    last.then_inc(S.lg_pe, 1)

            by_parity(pe, chunk_step)

        def norm_act(n, kind):
            S, D = ST[n], counts(n)
            act = nc.scalar
            act.wait_ge(S.stats_done, D.stats_done + 1)
            act.activation(LN[:, 3, :], LN[:, 2, :], ACT.Sqrt, scale=1.0 / H, bias=T.eps).then_inc(S.rstd_in, 1)

            def chunk_step(c, u):
                act.wait_ge(S.tr, D.tr + c + 1)
                if kind == "f0":
                    wait(act, S.lg_pe, c - 1, D.lg_pe)
                    act.activation(XTC[:, u, :], bank(u), ACT.Copy).then_inc(S.xt, 1)
                    act.activation(XHI[:, bass.ds(c * 512, 512)], bank(u), ACT.Copy).then_inc(S.xhi, 1)
                elif kind == "f1":
                    for h in range(2):
                        last = act.activation(XT[:, bass.ds((2 * c + h) * SEQ, SEQ)], bank(u)[:, h * SEQ:(h + 1) * SEQ],
                                              ACT.Copy, accum_out=POOL[:, bass.ds(2 * c + h, 1)])
                    last.then_inc(S.xt, 1)
                else:
                    act.activation(XT[:, bass.ds(c * 512, 512)], bank(u), ACT.Copy).then_inc(S.xt, 1)

            by_parity(act, chunk_step)

        POOL = T.pool
        XTC = XT[:, 0:1024].rearrange("p (u n) -> p u n", u=2)
        LG = AR[:, 0:NT * GC].rearrange("p (t e) -> p t e", t=NT)
        ar = lambda o, n: AR[:, o:o + n]
        o = NT * GC
        PR = ar(o, NT * E0).rearrange("p (t e) -> p t e", t=NT)
        EQ = ar(o + 256, NT * E0).rearrange("p (t e) -> p t e", t=NT)
        OH = ar(o + 512, NT * E0).rearrange("p (t e) -> p t e", t=NT)
        P2 = ar(o + 768, NT * E0).rearrange("p (t e) -> p t e", t=NT)
        T1 = ar(o + 1024, NT)
        T2 = ar(o + 1056, NT)
        SG = ar(o + 1088, NT)
        WALL = ar(o + 1120, NT * NG0).rearrange("p (t e) -> p t e", t=NT)
        WS = wstage.rearrange("p (u t e) -> p u t e", u=2, t=TPC)
        o2 = o + 1408
        SIL = ar(o2, 1024).rearrange("p (u n) -> p u n", u=2)
        PRD = ar(o2 + 1024, 1024).rearrange("p (u n) -> p u n", u=2)
        GAT = ar(o2 + 2048, 1024).rearrange("p (u n) -> p u n", u=2)
        ACC = ar(o2 + 3072, 512)
        HH = RR[:, 0:1024].rearrange("p (u n) -> p u n", u=2)
        HL = RR[:, 1024:2048].rearrange("p (u n) -> p u n", u=2)

        def bc(x, n):
            return x.unsqueeze(2).to_broadcast([P, NT, n])

        def f0_dve(n):
            S, D = ST[n], counts(n)
            v = nc.vector
            norm_dve(n, True)
            ch = Chain(v, S.gate_chain, D.gate_chain)
            v.wait_ge(S.lg_dve, D.lg_dve + NC)
            LE = LG[:, :, 0:E0]
            ch.link(v.tensor_reduce(T1, LE, AX.X, ALU.max))
            v.tensor_tensor(PR, LE, bc(T1, E0), ALU.subtract).then_inc(S.p_max, 1)
            v.wait_ge(S.p_exp, D.p_exp + 2)
            ch.link(v.tensor_reduce(T1, PR, AX.X, ALU.add))
            ch.link(v.reciprocal(T2, T1))
            ch.link(v.tensor_tensor(PR, PR, bc(T2, E0), ALU.mult))
            src = PR
            for k in range(TOP0):
                ch.link(v.tensor_reduce(T1, src, AX.X, ALU.max))
                ch.link(v.tensor_tensor(EQ, src, bc(T1, E0), ALU.is_equal))
                ch.link(v.tensor_tensor(EQ, EQ, rev.unsqueeze(1).to_broadcast([P, NT, E0]), ALU.mult))
                ch.link(v.tensor_reduce(T2, EQ, AX.X, ALU.max))
                ch.link(v.tensor_tensor(EQ, EQ, bc(T2, E0), ALU.is_equal))
                if k == 0:
                    ch.link(v.tensor_copy(OH, EQ))
                    ch.link(v.scalar_tensor_tensor(P2.rearrange("p t e -> p (t e)"), EQ.rearrange("p t e -> p (t e)"), -2.0,
                                                   PR.rearrange("p t e -> p (t e)"), ALU.mult, ALU.add))
                    src = P2
                else:
                    ch.link(v.tensor_tensor(OH, OH, EQ, ALU.add))
            ch.link(v.tensor_tensor(WALL[:, :, 0:E0], PR, OH, ALU.mult))
            ch.link(v.tensor_scalar(SG, SG, 1.0, None, ALU.add))
            ch.link(v.reciprocal(T1, SG))
            ch.link(v.tensor_copy(WALL[:, :, E0:NG0], T1.unsqueeze(2)))
            links[(stages[n], "gate_chain")] = ch.n

            def chunk_step(c, u):
                wait(v, S.wt_pe, c - 1, D.wt_pe)
                v.tensor_copy(WS[:, u, :, :], WALL[:, bass.ds(c * TPC, TPC), :]).then_inc(S.ws, 1)
                v.wait_ge(S.wt_hi, D.wt_hi + c + 1)
                v.tensor_tensor(WTS[32:32 + NG0, bass.ds(c * 512, 512)], bank(u)[0:NG0, :],
                                WTS[0:NG0, bass.ds(c * 512, 512)].bitcast(F32), ALU.subtract).then_inc(S.wt_lo, 1)

            by_parity(v, chunk_step)

            def low(c, m):
                k = MT0 * c + m
                v.wait_ge(S.h_hi, D.h_hi + k + 1)
                wait(v, S.down, k - 1, D.down)
                v.tensor_tensor(HL[:, m % 2, :], GAT[:, m % 2, :], HH[:, m % 2, :].bitcast(F32),
                                ALU.subtract).then_inc(S.h_lo, 1)

            def back(c):
                v.wait_ge(S.back, D.back + c + 1)
                xs = X[:, bass.ds(c * TPC, TPC), :]
                v.tensor_tensor(xs, xs, bank(7).rearrange("p (t h) -> p t h", t=TPC), ALU.add).then_inc(S.x_new, 1)
                v.wait_ge(S.x_new, D.x_new + c + 1)
                for t in range(TPC):
                    last = v.bn_stats(STAT[:, bass.ds(c * TPC + t, 1), :], X[:, bass.ds(c * TPC + t, 1), :])
                last.then_inc(S.st_new, 1)

            def chunk(c, first):
                for m in range(MT0):
                    k = MT0 * c + m
                    v.wait_ge(S.silu, D.silu + k + 1)
                    v.wait_ge(S.u_pe, D.u_pe + k + 1)
                    v.tensor_tensor(PRD[:, m % 2, :], SIL[:, m % 2, :], bank(2 + m % 2), ALU.mult).then_inc(S.prod, 1)
                    v.wait_ge(S.prod, D.prod + k + 1)
                    v.wait_ge(S.w_pe, D.w_pe + k + 1)
                    wait(v, S.h_hi, k - 1, D.h_hi)
                    v.tensor_tensor(GAT[:, m % 2, :], PRD[:, m % 2, :], bank(4 + m % 2), ALU.mult).then_inc(S.gated, 1)
                    if m > 0:
                        low(c, m - 1)
                    elif not first:
                        low(c - 1, MT0 - 1)
                    if m == 5 and not first:
                        back(c - 1)

            chunk(0, True)
            with v.Fori(1, NC) as c:
                chunk(c, False)
            low(NC - 1, MT0 - 1)
            back(NC - 1)

        def f0_act(n):
            S, D = ST[n], counts(n)
            act = nc.scalar
            norm_act(n, "f0")
            act.wait_ge(S.p_max, D.p_max + 1)
            act.activation(PR, PR, ACT.Exp).then_inc(S.p_exp, 1)
            act.wait_ge(S.lg_dve, D.lg_dve + NC)
            act.activation(SG, LG[:, :, E0], ACT.Exp, scale=-1.0).then_inc(S.p_exp, 1)

            def chunk_step(c, u):
                act.wait_ge(S.wt_pe, D.wt_pe + c + 1)
                act.activation(WTS[0:NG0, bass.ds(c * 512, 512)], bank(u)[0:NG0, :], ACT.Copy).then_inc(S.wt_hi, 1)

            by_parity(act, chunk_step)

            def high(c, m):
                k = MT0 * c + m
                act.wait_ge(S.gated, D.gated + k + 1)
                wait(act, S.down, k - 1, D.down)
                act.activation(HH[:, m % 2, :], GAT[:, m % 2, :], ACT.Copy).then_inc(S.h_hi, 1)

            def acc_copy(c):
                act.wait_ge(S.down, D.down + MT0 * c + MT0)
                wait(act, S.back, c, D.back)
                act.activation(ACC, bank(6), ACT.Copy, scale=0.5).then_inc(S.acc_copied, 1)

            def chunk(c, first):
                for m in range(MT0):
                    k = MT0 * c + m
                    act.wait_ge(S.g_pe, D.g_pe + k + 1)
                    wait(act, S.prod, k - 1, D.prod)
                    act.activation(SIL[:, m % 2, :], bank(m % 2), ACT.Silu).then_inc(S.silu, 1)
                    if m > 0:
                        high(c, m - 1)
                    elif not first:
                        high(c - 1, MT0 - 1)
                    if m == 2 and not first:
                        acc_copy(c - 1)

            chunk(0, True)
            with act.Fori(1, NC) as c:
                chunk(c, False)
            high(NC - 1, MT0 - 1)
            acc_copy(NC - 1)

        def f0_pe(n):
            S, D = ST[n], counts(n)
            pe = nc.tensor
            norm_pe(n, True)

            def chunk_step(c, u):
                pe.wait_ge(S.ws, D.ws + c + 1)
                wait(pe, S.wt_lo, c - 1, D.wt_lo)
                if u == 0:
                    pe.wait_ge(S.xlo, D.xlo + NC)
                for t in range(TPC):
                    last = pe.transpose(bank(u)[0:NG0, t * P:(t + 1) * P], WS[:, u, t, :], ident)
                last.then_inc(S.wt_pe, 1)

            by_parity(pe, chunk_step)
            pe.wait_ge(S.wt_lo, D.wt_lo + NC)
            pe.wait_ge(G.split, 1)

            def product(out, w, m, c, sem):
                for j, (i, x) in enumerate(((0, XHI), (0, XLO), (1, XHI))):
                    last = pe.matmul(out, w[i][:, m * P:(m + 1) * P], x[:, bass.ds(c * 512, 512)],
                                     start=(j == 0), stop=(j == 2))
                last.then_inc(sem, 1)

            def up(c, m):
                k = MT0 * c + m
                wait(pe, S.silu, k - 1, D.silu)
                product(bank(m % 2), WG, m, c, S.g_pe)
                wait(pe, S.prod, k - 1, D.prod)
                product(bank(2 + m % 2), WU, m, c, S.u_pe)
                wait(pe, S.gated, k - 1, D.gated)
                pe.matmul(bank(4 + m % 2), SEL[:, m * P:(m + 1) * P], WTS[:, bass.ds(c * 512, 512)],
                          start=True, stop=True).then_inc(S.w_pe, 1)

            def down(c, m):
                k = MT0 * c + m
                if m == 0:
                    wait(pe, S.acc_copied, c, D.acc_copied)
                pe.wait_ge(S.h_lo, D.h_lo + k + 1)
                for j, (i, h) in enumerate(((0, HH), (0, HL), (1, HH))):
                    last = pe.matmul(bank(6), WD[i][:, m, :], h[:, m % 2, :], start=(m == 0 and j == 0),
                                     stop=(m == MT0 - 1 and j == 2))
                last.then_inc(S.down, 1)

            def back(c):
                pe.wait_ge(S.acc_copied, D.acc_copied + c + 1)
                wait(pe, S.x_new, c, D.x_new)
                for t in range(TPC):
                    last = pe.transpose(bank(7)[:, t * P:(t + 1) * P], ACC[:, t * P:(t + 1) * P], ident)
                last.then_inc(S.back, 1)

            def chunk(c, first):
                for m in range(MT0):
                    up(c, m)
                    if m >= 2:
                        down(c, m - 2)
                    elif not first:
                        down(c - 1, MT0 - 2 + m)
                    if m == 3 and not first:
                        back(c - 1)

            chunk(0, True)
            with pe.Fori(1, NC) as c:
                chunk(c, False)
            down(NC - 1, MT0 - 2)
            down(NC - 1, MT0 - 1)
            back(NC - 1)

        def att(n):
            one = stages[n] == "a1"
            B = Buffers()
            B.one, B.S, B.nh = one, ST[n], NH1 if one else NH0
            B.nS = B.nh
            B.nG = B.nh // 4
            B.scale = SC1 if one else SC0
            B.PT = ar(0, 4096).rearrange("p (u k j q) -> p u k j q", u=2, k=2, j=4)
            B.OS = ar(4096, 1024)
            B.MM = ar(5120, 1024)
            B.MM1 = ar(5120, 32).rearrange("p (k r h) -> p k r h", k=2, r=2)
            B.KAP = ar(5376, SEQ)
            B.AO = ar(6144, 512)
            B.AOT = ar(6656, 512)
            B.MX = ar(7168, 32)
            B.RD = ar(7200, 32)
            B.KX = ar(7232, 256)
            B.KSF = ar(7488, 256)
            B.QX = XN.rearrange("p u t h -> p (u t h)")[:, 0:1024]
            B.MH = RR[:, 0:32]
            if one:
                B.KS = XHI.rearrange("p (u h k) -> p u h k", u=2, h=8)
                B.KH = XLO[:, 0:1024]
                B.QS = XLO[:, 1024:1536].rearrange("p (u q) -> p u q", u=2)
                B.QH = XLO[:, 1536:1792]
                B.MTC = XLO[:, 1792:2048]
                B.NEG = XLO[:, 2048:3072].rearrange("p (h k) -> p h k", h=8)
            else:
                B.QS = XHI[:, 0:2048].rearrange("p (u j q) -> p u j q", u=2, j=4)
                B.KS = XHI[:, 2048:4096].rearrange("p (u g k) -> p u g k", u=2, g=4)
                B.QH = XLO[:, 0:1024]
                B.QS2 = XLO[:, 1024:2048]
                B.KH = XLO[:, 2048:2304]
            return B

        def batches(eng, body):
            body(0, 0, True)
            with eng.Fori(0, (NB - 2) // 2) as i:
                body(2 * i + 1, 1, True)
                body(2 * i + 2, 0, True)
            body(NB - 1, (NB - 1) % 2, False)

        def att_pool(n):
            B = att(n)
            S = B.S
            g = nc.gpsimd
            sem, count = x_done(n)
            g.wait_ge(sem, count)
            if B.one:
                g.memset(B.MTC.bitcast(F32), 0.0).then_inc(S.zero, 1)
                g.wait_ge(S.zero, 1)
                g.wait_ge(S.prep_copy, 3)
                g.memset(B.KAP[DC1 + DR1:KAP, :], 1.0).then_inc(S.zero, 1)
            else:
                g.memset(B.MM, 0.0).then_inc(S.zero, 1)
            g.wait_ge(S.zero, 2 if B.one else 1)
            g.wait_ge(S.xt, NC)

            def copy(b, u):
                wait(g, S.kv if B.one else S.q, b - 1)
                g.tensor_copy(XTB[:, u, :], XT[:, bass.ds(b * SEQ, SEQ)]).then_inc(S.xtb, 1)

            copy(0, 0)
            copy(1, 1)
            with g.Fori(1, NB // 2) as i:
                copy(2 * i, 0)
                copy(2 * i + 1, 1)

        def att_pe(n):
            B = att(n)
            S = B.S
            pe = nc.tensor
            norm_pe(n, False)
            pe.wait_ge(S.xt, NC)
            if B.one:
                prep_pe(B)
                pe.wait_ge(S.negsel, 1)
            pe.wait_ge(S.zero, 2 if B.one else 1)

            def maxima(b):
                pe.wait_ge(S.mm, b + 1)
                wait(pe, S.ao, b)
                for k in range(2):
                    if B.one:
                        last = pe.transpose(bank(4)[0:16, k * P:(k + 1) * P], B.MM1[:, k, :, :].rearrange("p r h -> p (r h)"), ident)
                        continue
                    for j in range(4):
                        last = pe.transpose(bank(4, 2)[:, j * SEQ + k * P:j * SEQ + (k + 1) * P],
                                            B.MM[:, (k * 4 + j) * P:(k * 4 + j + 1) * P], ident)
                last.then_inc(S.mt, 1)

            def project(b, u):
                pe.wait_ge(S.xtb, b + 1)
                wait(pe, S.x_new, b - 1)
                wait(pe, S.aot, b - 1)
                x = XTB[:, u, :]
                if B.one:
                    pe.matmul(bank(6)[0:DC1 + DR1, 0:SEQ], T.wkap, x, start=True, stop=True)
                    pe.matmul(bank(6)[:, SEQ:2 * SEQ], T.wdqs, x, start=True, stop=True)
                else:
                    pe.matmul(bank(6)[:, 0:SEQ], T.wks, x, start=True, stop=True)
                for k in range(2):
                    last = pe.matmul(bank(7)[:, k * 32:(k + 1) * 32], x[:, k * P:(k + 1) * P], T.wckv if B.one else T.wv,
                                     start=True, stop=True)
                last.then_inc(S.kv, 1)
                if B.one:
                    return
                wait(pe, S.qs2, b)
                for j in range(4):
                    last = pe.matmul(bank(4, 2)[:, j * SEQ:(j + 1) * SEQ], T.wqs[:, j * P:(j + 1) * P], x, start=True, stop=True)
                last.then_inc(S.q, 1)

            def head_keys(b, r):
                if r == 0:
                    pe.wait_ge(S.kx, b + 1)
                    wait(pe, S.mtc, b)
                else:
                    pe.wait_ge(S.kp_lo, 2 * b + r)
                for j in range(4):
                    last = pe.matmul(bank(4, 2)[:, j * SEQ:(j + 1) * SEQ], bs1[0:KAP, (4 * r + j) * P:(4 * r + j + 1) * P],
                                     B.KAP[0:KAP, :], start=True, stop=True)
                last.then_inc(S.kp_pe, 1)

            def scores(b, u, m):
                if m == 0:
                    pe.wait_ge(S.qs, b + 1)
                    if B.one:
                        pe.wait_ge(S.kp_lo, 2 * b + 2)
                    else:
                        pe.wait_ge(S.ksz, b + 1)
                wait(pe, S.smax, B.nS * b + m - 1)
                if B.one:
                    k, hp = divmod(m, 4)
                    lhs, rhs = B.QS[:, u, k * P:(k + 1) * P], B.KS[:, u, 2 * hp:2 * hp + 2, :]
                else:
                    k, j, gp = m // 8, m // 2 % 4, m % 2
                    lhs, rhs = B.QS[:, u, j, k * P:(k + 1) * P], B.KS[:, u, 2 * gp:2 * gp + 2, :]
                pe.matmul(bank(m % 2), lhs, rhs, start=True, stop=True).then_inc(S.s_pe, 1)

            def scores_t(b, u, m):
                if m == 0:
                    pe.wait_ge(S.mtc if B.one else S.qs2, b + 1)
                wait(pe, S.exp, B.nS * b + m - 1)
                if B.one:
                    hp, k = divmod(m, 2)
                    for i in range(2):
                        o = bank(2 + m % 2)[:, i * SEQ:(i + 1) * SEQ]
                        pe.matmul(o, B.KS[:, u, 2 * hp + i, k * P:(k + 1) * P], B.QS[:, u, :], start=True, stop=False)
                        last = pe.matmul(o, B.NEG[:, 2 * hp + i, :], B.MTC, start=False, stop=True)
                    last.then_inc(S.st_pe, 1)
                else:
                    g, k, jp = m // 4, m // 2 % 2, m % 2
                    pe.matmul(bank(2 + m % 2), B.KS[:, u, g, k * P:(k + 1) * P], B.QS2[:, jp * 512:(jp + 1) * 512],
                              start=True, stop=True).then_inc(S.st_pe, 1)

            def values(b, u, g, more):
                pe.wait_ge(S.exp, B.nS * b + 4 * g + 4)
                if g == 0:
                    pe.wait_ge(S.v, b + (2 if more else 1))
                    pe.wait_ge(S.kx, b + (2 if more else 1))
                    if B.one and more:
                        pe.wait_ge(S.qh, b + 2)
                    wait(pe, S.x_new, b)
                    wait(pe, S.aot, b)
                for k in range(2):
                    for j in range(4):
                        if B.one:
                            pe.matmul(bank(6)[32 * j:32 * j + 32, g * SEQ:(g + 1) * SEQ], VA[:, u, k, 0, :], B.PT[:, g % 2, k, j, :],
                                      start=(k == 0), stop=(k == 1), skip_group_check=True)
                        else:
                            last = pe.matmul(bank(6, 2)[32 * j:32 * j + 32, g * SEQ:(g + 1) * SEQ], VA[:, u, k, g, :],
                                             B.PT[:, g % 2, k, j, :], start=(k == 0), stop=(k == 1), skip_group_check=True)
                if B.one:
                    for k in range(2):
                        for j in range(4):
                            last = pe.matmul(bank(7)[32 * j:32 * j + 32, g * SEQ:(g + 1) * SEQ], ones[:, 0:32],
                                             B.PT[:, g % 2, k, j, :], start=(k == 0), stop=(k == 1), skip_group_check=True)
                last.then_inc(S.av, 1)

            def turn(b, more):
                pe.wait_ge(S.os, b + 1)
                if more:
                    if B.one:
                        pe.wait_ge(S.kp_lo, 2 * b + 4)
                    else:
                        pe.wait_ge(S.qx, b + 2)
                for k in range(2):
                    for g in range(4):
                        last = pe.transpose(bank(4 + k)[:, g * P:(g + 1) * P], B.OS[:, g * SEQ + k * P:g * SEQ + (k + 1) * P], ident)
                last.then_inc(S.ot, 1)

            def turn_back(b):
                pe.wait_ge(S.ao, b + 1)
                n_ = 2 if B.one else 1
                for g in range(n_):
                    for k in range(2):
                        last = pe.transpose(bank(6)[:, g * SEQ + k * P:g * SEQ + (k + 1) * P],
                                            B.AO[:, (k * n_ + g) * P:(k * n_ + g + 1) * P], ident)
                last.then_inc(S.aot_pe, 1)

            def project_out(b):
                pe.wait_ge(S.aot, b + 1)
                for k in range(2):
                    o = bank(7)[:, k * P:(k + 1) * P]
                    if B.one:
                        for g in range(2):
                            pe.matmul(o, B.AOT[:, g * SEQ + k * P:g * SEQ + (k + 1) * P], cg[:, g * H:(g + 1) * H],
                                      start=(g == 0), stop=False)
                    else:
                        pe.matmul(o, B.AOT[:, k * P:(k + 1) * P], T.wo, start=True, stop=False)
                    last = pe.matmul(o, ones[0:1, :], (cb if B.one else T.bo)[0:1, :], start=False, stop=True)
                last.then_inc(S.out, 1)

            def body(b, u, more):
                w = 1 - u
                maxima(b)
                if more:
                    project(b + 1, w)
                if B.one:
                    scores_t(b, u, 0)
                    scores_t(b, u, 1)
                    if more:
                        head_keys(b + 1, 0)
                    scores_t(b, u, 2)
                    scores_t(b, u, 3)
                    if more:
                        head_keys(b + 1, 1)
                    plan = [("t", 4), ("t", 5), ("v", 0), ("s", 0), ("t", 6), ("s", 1), ("t", 7), ("s", 2), ("s", 3), ("v", 1),
                            ("s", 4), ("s", 5), ("turn", 0), ("s", 6), ("back", 0), ("s", 7), ("out", 0)]
                else:
                    for m in range(4):
                        scores_t(b, u, m)
                    plan = []
                    for m in range(12):
                        plan += [("s", m), ("t", m + 4)]
                        if m % 4 == 1:
                            plan.append(("v", m // 4))
                    plan += [("s", 12), ("v", 3), ("s", 13), ("s", 14), ("turn", 0), ("s", 15), ("back", 0), ("out", 0)]
                for what, m in plan:
                    if what == "t":
                        scores_t(b, u, m)
                    elif what == "s" and more:
                        scores(b + 1, w, m)
                    elif what == "v":
                        values(b, u, m, more)
                    elif what == "turn":
                        turn(b, more)
                    elif what == "back":
                        turn_back(b)
                    elif what == "out":
                        project_out(b)

            project(0, 0)
            if B.one:
                head_keys(0, 0)
                head_keys(0, 1)
            for m in range(B.nS):
                scores(0, 0, m)
            batches(pe, body)

        def att_act(n):
            B = att(n)
            S = B.S
            act = nc.scalar
            norm_act(n, "a")
            if B.one:
                prep_act(B)

            def keys(b):
                act.wait_ge(S.kv, b + 1)
                if B.one:
                    wait(act, S.kp_pe, 2 * b)
                    act.activation(B.KAP[0:DC1 + DR1, :], bank(6)[0:DC1 + DR1, 0:SEQ], ACT.Identity, bias=T.b1k[0:DC1 + DR1, :])\
                        .then_inc(S.kx, 1)
                    wait(act, S.qs, b)
                    act.activation(B.QX[:, 0:SEQ], bank(6)[:, SEQ:2 * SEQ], ACT.Identity, bias=T.b1q)
                    act.activation(B.QH, bank(6)[:, SEQ:2 * SEQ], ACT.Identity, bias=T.b1q).then_inc(S.qh, 1)
                else:
                    wait(act, S.ksz, b)
                    act.activation(B.KX, bank(6)[:, 0:SEQ], ACT.Identity, bias=T.bqk[:, 4:5])
                    act.activation(B.KH, bank(6)[:, 0:SEQ], ACT.Identity, bias=T.bqk[:, 4:5]).then_inc(S.kx, 1)

            def queries(b):
                act.wait_ge(S.q, b + 1)
                wait(act, S.qs, b)
                for j in range(4):
                    last = act.activation(B.QX[:, j * SEQ:(j + 1) * SEQ], bank(4, 2)[:, j * SEQ:(j + 1) * SEQ], ACT.Identity,
                                          bias=T.bqk[:, j:j + 1])
                last.then_inc(S.qx, 1)
                act.wait_ge(S.qx, b + 1)
                act.activation(B.QH, B.QX, ACT.Copy).then_inc(S.qh, 1)

            def head_keys(b, r):
                act.wait_ge(S.kp_pe, 2 * b + r + 1)
                wait(act, S.kp_lo, 2 * b + r)
                act.activation(B.KH, bank(4, 2), ACT.Copy).then_inc(S.kp_hi, 1)

            def exps(b, m):
                act.wait_ge(S.st_pe, B.nS * b + m + 1)
                if m % 4 == 0:
                    wait(act, S.av, B.nG * b + m // 4 - 1)
                if B.one:
                    hp, k = divmod(m, 2)
                    o = B.PT[:, hp // 2, k, hp % 2 * 2:hp % 2 * 2 + 2, :]
                else:
                    g, k, jp = m // 4, m // 2 % 2, m % 2
                    o = B.PT[:, g % 2, k, 2 * jp:2 * jp + 2, :]
                act.activation(o, bank(2 + m % 2).rearrange("p (j q) -> p j q", j=2), ACT.Exp, scale=B.scale).then_inc(S.exp, 1)

            def body(b, u, more):
                if B.one:
                    act.wait_ge(S.mt, b + 1)
                    wait(act, S.st_pe, B.nS * b)
                    act.activation(B.MTC[0:16, :], bank(4)[0:16, 0:SEQ], ACT.Copy).then_inc(S.mtc, 1)
                if more:
                    keys(b + 1)
                for m in range(B.nS):
                    exps(b, m)
                    if m == 1 and more:
                        if B.one:
                            head_keys(b + 1, 0)
                        else:
                            queries(b + 1)
                    if m == 3 and more and B.one:
                        head_keys(b + 1, 1)
                act.wait_ge(S.av, B.nG * b + B.nG)
                wait(act, S.ot, b)
                act.activation(B.OS, bank(6, 2), ACT.Copy).then_inc(S.os, 1)
                act.wait_ge(S.aot_pe, b + 1)
                wait(act, S.out, b)
                w_ = 512 if B.one else SEQ
                act.activation(B.AOT[:, 0:w_], bank(6)[:, 0:w_], ACT.Copy).then_inc(S.aot, 1)

            keys(0)
            if B.one:
                head_keys(0, 0)
                head_keys(0, 1)
            else:
                queries(0)
            batches(act, body)

        def att_dve(n):
            B = att(n)
            S = B.S
            v = nc.vector
            norm_dve(n, False)
            if B.one:
                prep_dve(B)
            rchain = Chain(v, S.r_chain)
            mchain = Chain(v, S.m_chain)
            kchain = None if B.one else Chain(v, S.k_chain)

            def vals(b, u):
                v.wait_ge(S.kv, b + 1)
                wait(v, S.av, B.nG * (b - 1))
                if B.one:
                    v.tensor_tensor(VA[:, u, :, 0, :], bank(7)[:, 0:64].rearrange("p (k d) -> p k d", k=2),
                                    T.bckv.unsqueeze(1).to_broadcast([P, 2, 32]), ALU.add).then_inc(S.v, 1)
                    return
                for k in range(2):
                    last = v.tensor_tensor(VA[:, u, k, :, 0:HD0], bank(7)[:, k * 32:(k + 1) * 32].rearrange("p (g d) -> p g d", g=4),
                                           T.bvb.rearrange("p (g d) -> p g d", g=4), ALU.add)
                last.then_inc(S.v, 1)

            def stacks(b, u):
                v.wait_ge(S.qh, b + 1)
                if B.one:
                    v.scalar_tensor_tensor(B.QS[:, u, :], B.QH.bitcast(F32), T.masks[:, 6:7], B.QX[:, 0:SEQ], ALU.mult, ALU.add)\
                        .then_inc(S.qs, 1)
                    return
                v.scalar_tensor_tensor(B.QS[:, u, :, :].rearrange("p j q -> p (j q)"), B.QH.bitcast(F32), T.masks[:, 0:1], B.QX,
                                       ALU.mult, ALU.add).then_inc(S.qs, 1)

            def key_stacks(b, u):
                v.wait_ge(S.kx, b + 1)
                kchain.base, kchain.n = b, 0
                kchain.link(v.scalar_tensor_tensor(B.KSF, B.KH.bitcast(F32), T.masks[:, 1:2], B.KX, ALU.mult, ALU.add))
                for g in range(4):
                    last = v.tensor_scalar(B.KS[:, u, g, :], B.KSF, T.masks[:, 2 + g:3 + g], None, ALU.mult)
                last.then_inc(S.ksz, 1)

            def head_keys(b, u, r):
                v.wait_ge(S.kp_hi, 2 * b + r + 1)
                v.scalar_tensor_tensor(B.KS[:, u, 4 * r:4 * r + 4, :].rearrange("p h k -> p (h k)"), B.KH.bitcast(F32),
                                       T.masks[:, 7:8], bank(4, 2), ALU.mult, ALU.add).then_inc(S.kp_lo, 1)

            def smax(b, m):
                v.wait_ge(S.s_pe, B.nS * b + m + 1)
                v.tensor_reduce(B.MX[:, 2 * m:2 * m + 2], bank(m % 2).rearrange("p (h k) -> p h k", h=2), AX.X, ALU.max)\
                    .then_inc(S.smax, 1)

            def maxima(b):
                v.wait_ge(S.smax, B.nS * (b + 1))
                wait(v, S.mt, b)
                mchain.base, mchain.n = b, 0
                n_ = 2 * B.nS
                mchain.link(v.tensor_copy(B.MH[:, 0:n_], B.MX[:, 0:n_]))
                if B.one:
                    hi, lo = B.MM1[:, :, 0, :], B.MM1[:, :, 1, :]
                    mh, mx = (z[:, 0:n_].rearrange("p (k h) -> p k h", k=2) for z in (B.MH.bitcast(F32), B.MX))
                else:
                    mm = B.MM.rearrange("p (n c) -> p n c", c=32)
                    hi, lo = mm[:, :, 24], mm[:, :, 25]
                    mh, mx = B.MH.bitcast(F32), B.MX
                v.tensor_copy(hi, mh)
                v.tensor_tensor(lo, mx, mh, ALU.subtract).then_inc(S.mm, 1)

            def normalise(b):
                v.wait_ge(S.ot, b + 1)
                wait(v, S.aot_pe, b)
                rchain.base, rchain.n = b, 0
                if B.one:
                    t = bank(4, 2).rearrange("p (k x j i) -> p k x j i", k=2, x=4, j=4)
                    for k in range(2):
                        last = v.reciprocal(B.RD[:, k * 8:(k + 1) * 8], bank(4 + k)[:, 256:512].rearrange("p (x i) -> p x i", i=32)[:, :, 0])
                    rchain.link(last)
                    for k in range(2):
                        last = v.tensor_tensor(B.AO[:, k * 256:(k + 1) * 256].rearrange("p (x i) -> p x i", i=32),
                                               bank(4 + k)[:, 0:256].rearrange("p (x i) -> p x i", i=32),
                                               B.RD[:, k * 8:(k + 1) * 8].unsqueeze(2).to_broadcast([P, 8, 32]), ALU.mult)
                else:
                    for k in range(2):
                        last = v.reciprocal(B.RD[:, k * 16:(k + 1) * 16], bank(4 + k).rearrange("p (x i) -> p x i", i=32)[:, :, HD0])
                    rchain.link(last)
                    for k in range(2):
                        last = v.tensor_tensor(B.AO[:, k * P:(k + 1) * P].rearrange("p (x i) -> p x i", i=HD0),
                                               bank(4 + k).rearrange("p (x i) -> p x i", i=32)[:, :, 0:HD0],
                                               B.RD[:, k * 16:(k + 1) * 16].unsqueeze(2).to_broadcast([P, 16, HD0]), ALU.mult)
                last.then_inc(S.ao, 1)

            def add(b):
                v.wait_ge(S.out, b + 1)
                xs = X[:, bass.ds(b * TPB, TPB), :]
                v.tensor_tensor(xs, xs, bank(7)[:, 0:TPB * H].rearrange("p (t h) -> p t h", t=TPB), ALU.add).then_inc(S.x_new, 1)
                v.wait_ge(S.x_new, b + 1)
                for t in range(TPB):
                    last = v.bn_stats(STAT[:, bass.ds(b * TPB + t, 1), :], X[:, bass.ds(b * TPB + t, 1), :])
                last.then_inc(S.st_new, 1)

            def body(b, u, more):
                w = 1 - u
                if not B.one:
                    v.wait_ge(S.mt, b + 1)
                    wait(v, S.st_pe, B.nS * b)
                    v.tensor_tensor(B.QS2, B.QS[:, u, :, :].rearrange("p j q -> p (j q)").bitcast(F32), bank(4, 2), ALU.add)\
                        .then_inc(S.qs2, 1)
                if more:
                    vals(b + 1, w)
                    if B.one:
                        stacks(b + 1, w)
                        head_keys(b + 1, w, 0)
                        head_keys(b + 1, w, 1)
                    else:
                        key_stacks(b + 1, w)
                        stacks(b + 1, w)
                    for m in range(B.nS - 1):
                        smax(b + 1, m)
                normalise(b)
                if more:
                    smax(b + 1, B.nS - 1)
                    maxima(b + 1)
                add(b)

            vals(0, 0)
            if B.one:
                stacks(0, 0)
                head_keys(0, 0, 0)
                head_keys(0, 0, 1)
            else:
                key_stacks(0, 0)
                stacks(0, 0)
            for m in range(B.nS):
                smax(0, m)
            v.wait_ge(S.zero, 1)
            maxima(0)
            batches(v, body)

        RAW1 = ar(0, 0 + RAW1_N)

        def prep_views():
            at, out_ = 0, {}
            for name, n in RAW1_PARTS.items():
                out_[name] = RAW1[:, at:at + n]
                at += n
            return names(out_)

        def prep_pe(B):
            S = B.S
            pe = nc.tensor
            R = prep_views()
            pe.wait_ge(S.raw_in, 16)
            for r in range(2):
                for j in range(4):
                    h = 4 * r + j
                    o = bank(r)[0:KAP, j * P:(j + 1) * P]
                    pe.matmul(o, R.ukt[:, h * KAP:(h + 1) * KAP], R.uqt[:, h * P:(h + 1) * P], start=True, stop=False)
                    last = pe.matmul(o, R.qrp[0:DC1 + 1, h * KAP:(h + 1) * KAP], R.spread[0:DC1 + 1, :], start=False, stop=True)
            for g in range(2):
                for j in range(4):
                    h = 4 * g + j
                    last = pe.matmul(bank(2)[:, g * H:(g + 1) * H], R.uvt[:, h * P:(h + 1) * P], R.wo[:, h * H:(h + 1) * H],
                                     start=(j == 0), stop=(j == 3))
            for h in range(NH1):
                pe.matmul(bank(3)[0:1, 0:H], R.buv[:, h:h + 1], R.wo[:, h * H:(h + 1) * H], start=(h == 0), stop=False)
            pe.matmul(bank(3)[0:1, 0:H], ones[0:1, 0:1], T.bo1[0:1, :], start=False, stop=True).then_inc(S.prep_pe, 1)

        def prep_act(B):
            S = B.S
            act = nc.scalar
            act.wait_ge(S.prep_pe, 1)
            act.activation(bs1[0:KAP, 0:512], bank(0)[0:KAP, :], ACT.Copy)
            act.activation(bs1[0:KAP, 512:1024], bank(1)[0:KAP, :], ACT.Copy).then_inc(S.prep_copy, 1)
            act.activation(cg, bank(2)[:, 0:2 * H], ACT.Copy).then_inc(S.prep_copy, 1)
            act.activation(cb[0:1, :], bank(3)[0:1, 0:H], ACT.Copy).then_inc(S.prep_copy, 1)

        def prep_dve(B):
            S = B.S
            v = nc.vector
            R = prep_views()
            v.wait_ge(S.raw_in, 16)
            v.tensor_copy(B.NEG.rearrange("p h k -> p (h k)"), R.neg).then_inc(S.negsel, 1)
        HS = ar(0, 3072).rearrange("p (s m q) -> p s m q", s=TOP1, m=FT1)
        WA = ar(3072, 1536).rearrange("p (s n) -> p s n", s=TOP1)
        WB = ar(4608, 1536).rearrange("p (s m n) -> p s m n", s=TOP1, m=FT1)
        SUMT = ar(6144, SEQ)
        TH = ar(6400, NB)
        LR = ar(6416, E1)
        R1 = ar(6424, 1)
        R2 = ar(6425, 1)
        EQR = ar(6432, E1)
        TOPV = ar(6440, TOP1)
        TOPI = ar(6448, TOP1)
        DD = ar(6456, 2 * NB * TOP1).rearrange("p (a b k) -> p a b k", a=2, b=NB)
        W48 = ar(6552, NB * TOP1)
        R5, N5 = LN[:, 0, :], LN[:, 1, :]

        def f1_sp(n):
            S, D = ST[n], counts(n)
            sp = nc.sync
            sp.wait_ge(S.idx, D.idx + 1)

            def fetch(b):
                for k in range(TOP1):
                    wait(sp, S.z_pe, TOP1 * (b - 1) + k + 1, D.z_pe)
                    e = sp.value_load(IDX[0:1, bass.ds(b * TOP1 + k, 1)], min_val=0, max_val=E1 - 1)
                    sem = (S.w_in0, S.w_in1, S.w_in2)[k]
                    sp.dma_start(WA[:, k:k + 1, :], a.zone_up.rearrange("e p n -> p e n")[:, bass.ds(e, 1), :]).then_inc(sem, 16)
                    sp.dma_start(WB[:, k:k + 1, :, :].rearrange("p s m n -> p s (m n)"),
                                 a.zone_down.rearrange("e p n -> p e n")[:, bass.ds(e, 1), :]).then_inc(sem, 16)

            fetch(0)
            with sp.Fori(1, NB) as b:
                fetch(b)

        def f1_pe(n):
            S, D = ST[n], counts(n)
            pe = nc.tensor
            norm_pe(n, False)
            pe.wait_ge(S.xt, D.xt + NC)
            pe.matmul(bank(2)[0:RH1, 0:NB], T.w1, POOL, start=True, stop=True).then_inc(S.r_pe, 1)
            pe.wait_ge(S.r_act, D.r_act + 1)
            pe.matmul(bank(2)[0:NB, 32:32 + E1], TH[0:RH1, :], T.w2[0:RH1, :], start=True, stop=True).then_inc(S.r_pe, 1)
            pe.wait_ge(S.r_dve, D.r_dve + 1)
            pe.matmul(bank(2)[:, 64:64 + 2 * NB * TOP1], ones[0:NB, :], DD[0:NB, :, :, :], start=True, stop=True).then_inc(S.r_pe, 1)
            pe.wait_ge(S.idx, D.idx + 1)

            def up(b, k):
                pe.wait_ge((S.w_in0, S.w_in1, S.w_in2)[k], D.w_in0 + 32 * (b + 1))
                wait(pe, S.gelu, 6 * b + (0, -2, 2)[k], D.gelu)
                for m in range(FT1):
                    last = pe.matmul(bank(k % 2 * 2 + m // 2)[:, m % 2 * SEQ:(m % 2 + 1) * SEQ], WA[:, k, m * P:(m + 1) * P],
                                     XT[:, bass.ds(b * SEQ, SEQ)], start=True, stop=True)
                    if m % 2:
                        last.then_inc(S.u_pe, 1)

            def down(b, k):
                pe.wait_ge(S.gelu, D.gelu + 6 * b + 2 * k + 2)
                if k == 0:
                    wait(pe, S.sum, b, D.sum)
                for m in range(FT1):
                    last = pe.matmul(bank(4 + k)[:, 0:SEQ], WB[:, k, m, :], HS[:, k, m, :], start=(m == 0), stop=(m == FT1 - 1))
                last.then_inc(S.z_pe, 1)

            def back(b):
                pe.wait_ge(S.sum, D.sum + b + 1)
                wait(pe, S.x_half, b, D.x_half)
                for t in range(TPB):
                    last = pe.transpose(bank(7)[:, t * P:(t + 1) * P], SUMT[:, t * P:(t + 1) * P], ident)
                last.then_inc(S.back, 1)

            def batch(b, first):
                up(b, 0)
                if not first:
                    down(b - 1, 2)
                up(b, 1)
                down(b, 0) if first else None
                if not first:
                    back(b - 1)
                    down(b, 0)
                up(b, 2)
                down(b, 1)

            batch(0, True)
            with pe.Fori(1, NB) as b:
                batch(b, False)
            down(NB - 1, 2)
            back(NB - 1)

        def f1_act(n):
            S, D = ST[n], counts(n)
            act = nc.scalar
            norm_act(n, "f1")
            act.wait_ge(S.r_pe, D.r_pe + 1)
            act.activation(TH[0:RH1, :], bank(2)[0:RH1, 0:NB], ACT.Tanh, scale=1.0 / SEQ, bias=T.b1[0:RH1, :]).then_inc(S.r_act, 1)
            act.wait_ge(S.sub, D.sub + 1)
            act.activation(LR[0:NB, :], LR[0:NB, :], ACT.Exp).then_inc(S.r_act, 1)

            def batch(b):
                for k in range(TOP1):
                    for h in range(2):
                        act.wait_ge(S.u_pe, D.u_pe + 6 * b + 2 * k + h + 1)
                        if h == 0:
                            wait(act, S.z_pe, TOP1 * (b - 1) + k + 1, D.z_pe)
                        act.activation(HS[:, k, 2 * h:2 * h + 2, :], bank(k % 2 * 2 + h).rearrange("p (m q) -> p m q", m=2),
                                       ACT.Gelu_apprx_tanh).then_inc(S.gelu, 1)

            batch(0)
            with act.Fori(1, NB) as b:
                batch(b)

        def f1_dve(n):
            S, D = ST[n], counts(n)
            v = nc.vector
            norm_dve(n, False)
            ch = Chain(v, S.rt_chain, D.rt_chain)
            ch.link(v.tensor_scalar(R5, RSTD, 0.5, 1.0, ALU.mult, ALU.add))
            ch.link(v.tensor_scalar(N5, NBIAS, 0.5, None, ALU.mult))
            r = slice(0, NB)
            v.wait_ge(S.r_pe, D.r_pe + 2)
            ch.link(v.tensor_tensor(LR[r], bank(2)[r, 32:32 + E1], T.b2[r], ALU.add))
            ch.link(v.tensor_reduce(R1[r], LR[r], AX.X, ALU.max))
            v.tensor_scalar(LR[r], LR[r], R1[r], None, ALU.subtract).then_inc(S.sub, 1)
            v.wait_ge(S.r_act, D.r_act + 2)
            ch.link(v.tensor_reduce(R1[r], LR[r], AX.X, ALU.add))
            ch.link(v.reciprocal(R2[r], R1[r]))
            ch.link(v.tensor_scalar(LR[r], LR[r], R2[r], None, ALU.mult))
            for k in range(TOP1):
                tv, ti = TOPV[r, k:k + 1], TOPI[r, k:k + 1]
                ch.link(v.tensor_reduce(tv, LR[r], AX.X, ALU.max))
                ch.link(v.scalar_tensor_tensor(EQR[r], LR[r], tv, rev[r], ALU.is_equal, ALU.mult))
                ch.link(v.tensor_reduce(ti, EQR[r], AX.X, ALU.max))
                ch.link(v.tensor_scalar(EQR[r], EQR[r], ti, -2.0, ALU.is_equal, ALU.mult))
                if k < TOP1 - 1:
                    ch.link(v.tensor_tensor(LR[r], LR[r], EQR[r], ALU.add))
            ch.link(v.tensor_reduce(R1[r], TOPV[r], AX.X, ALU.add))
            ch.link(v.reciprocal(R2[r], R1[r]))
            ch.link(v.tensor_scalar(TOPV[r], TOPV[r], R2[r], 0.5, ALU.mult, ALU.mult))
            ch.link(v.tensor_scalar(TOPI[r], TOPI[r], -1.0, float(E1), ALU.mult, ALU.add))
            for i, x in enumerate((TOPV, TOPI)):
                last = v.tensor_tensor(DD[r, i, :, :], T.diag[r].unsqueeze(2).to_broadcast([NB, NB, TOP1]),
                                       x[r].unsqueeze(1).to_broadcast([NB, NB, TOP1]), ALU.mult)
            last.then_inc(S.r_dve, 1)
            v.wait_ge(S.r_pe, D.r_pe + 3)
            n_ = NB * TOP1
            v.tensor_copy(W48, bank(2)[:, 64:64 + n_])
            ch.link(v.tensor_copy(IDX[:, :], bank(2)[:, 64 + n_:64 + 2 * n_]))
            v.tensor_copy(EQR[r], rev[r]).then_inc(S.idx, 1)
            links[(stages[n], "rt_chain")] = ch.n

            def batch(b):
                v.wait_ge(S.z_pe, D.z_pe + TOP1 * (b + 1))
                wait(v, S.back, b, D.back)
                ac = Chain(v, S.acc_chain, D.acc_chain)
                ac.base = 2 * b
                w = [W48[:, bass.ds(b * TOP1 + k, 1)] for k in range(TOP1)]
                ac.link(v.tensor_scalar(SUMT, bank(4)[:, 0:SEQ], w[0], None, ALU.mult))
                ac.link(v.scalar_tensor_tensor(SUMT, bank(5)[:, 0:SEQ], w[1], SUMT, ALU.mult, ALU.add))
                v.scalar_tensor_tensor(SUMT, bank(6)[:, 0:SEQ], w[2], SUMT, ALU.mult, ALU.add).then_inc(S.sum, 1)
                v.wait_ge(S.back, D.back + b + 1)
                ts = [bass.ds(b * TPB + t, 1) for t in range(TPB)]
                for t in range(TPB):
                    last = v.scalar_tensor_tensor(X[:, ts[t], :], X[:, ts[t], :], R5[:, ts[t]],
                                                  bank(7)[:, t * H:(t + 1) * H].unsqueeze(1), ALU.mult, ALU.add)
                last.then_inc(S.x_half, 1)
                v.wait_ge(S.x_half, D.x_half + b + 1)
                for t in range(TPB):
                    last = v.tensor_scalar(X[:, ts[t], :], X[:, ts[t], :], N5[:, ts[t]], None, ALU.add)
                last.then_inc(S.x_new, 1)
                v.wait_ge(S.x_new, D.x_new + b + 1)
                for t in range(TPB):
                    last = v.bn_stats(STAT[:, ts[t], :], X[:, ts[t], :])
                last.then_inc(S.st_new, 1)

            batch(0)
            with v.Fori(1, NB) as b:
                batch(b)

        RAW = ar(2048, 3 * MT0 * P)
        RAWS = XT[:, 1024:1024 + MT0 * P]

        @block.sync
        def _(sp):
            xv = a.x.rearrange("b (t p) h -> p (b t) h", p=P)
            for q in range(4):
                sp.dma_start(X[:, q * 8:(q + 1) * 8, :], xv[:, q * 8:(q + 1) * 8, :]).then_inc(G.x_in, 16)
            sp.dma_start(SM[:, 0:SMALL_N], a.small).then_inc(G.small_in, 16)
            sp.dma_start(RAW, a.w0).then_inc(G.raw_in, 16)
            sp.dma_start(RAWS, a.sel).then_inc(G.raw_in, 16)
            for n, kind in enumerate(stages):
                if kind == "f1":
                    f1_sp(n)
                if kind == "a1":
                    sem, count = x_done(n)
                    sp.wait_ge(sem, count)
                    sp.dma_start(RAW1, a.w1).then_inc(ST[n].raw_in, 16)
            L = ST[-1]
            ov = out.rearrange("b (t p) h -> p (b t) h", p=P)
            for q in range(4):
                sp.wait_ge(L.x_new, counts(len(stages) - 1).x_new + runs[stages[-1]] // 4 * (q + 1))
                sp.dma_start(ov[:, q * 8:(q + 1) * 8, :], X[:, q * 8:(q + 1) * 8, :]).then_inc(G.out_done, 16)
            sp.wait_ge(G.out_done, 64)

        @block.gpsimd
        def _(g):
            g.wait_ge(G.small_in, 16)
            g.memset(WTS[:, :].bitcast(F32), 0.0)
            g.memset(VA, 0.0).then_inc(G.zeroed, 1)
            g.wait_ge(G.zeroed, 1)
            g.memset(VA[:, :, :, :, HD0:HD0 + 1], 1.0).then_inc(G.zeroed, 1)
            g.wait_ge(G.raw_in, 32)
            w = MT0 * P
            g.tensor_copy(SEL[:, :], RAWS)
            for i, W in enumerate((WG, WU, WD)):
                o = W[0].rearrange("p m h -> p (m h)") if i == 2 else W[0][:, :]
                last = g.tensor_copy(o, RAW[:, i * w:(i + 1) * w])
            last.then_inc(G.zeroed, 1)
            g.wait_ge(G.zeroed, 3)
            for i, W in enumerate((WG, WU, WD)):
                hi, lo = (W[j].rearrange("p m h -> p (m h)") if i == 2 else W[j][:, :] for j in range(2))
                last = g.tensor_tensor(lo, RAW[:, i * w:(i + 1) * w], hi.bitcast(F32), ALU.subtract)
            last.then_inc(G.split, 1)
            for n, kind in enumerate(stages):
                if kind in ("a0", "a1"):
                    att_pool(n)

        @block.scalar
        def _(act):
            act.wait_ge(G.small_in, 16)
            act.wait_ge(G.zeroed, 2)
            for n, kind in enumerate(stages):
                {"f0": f0_act, "f1": f1_act, "a0": att_act, "a1": att_act}[kind](n)

        @block.tensor
        def _(pe):
            pe.wait_ge(G.small_in, 16)
            for n, kind in enumerate(stages):
                {"f0": f0_pe, "f1": f1_pe, "a0": att_pe, "a1": att_pe}[kind](n)

        @block.vector
        def _(v):
            v.wait_ge(G.x_in, 64)
            v.wait_ge(G.small_in, 16)
            with v.Fori(0, NC) as c:
                for t in range(TPC):
                    last = v.bn_stats(STAT[:, bass.ds(c * TPC + t, 1), :], X[:, bass.ds(c * TPC + t, 1), :])
                last.then_inc(G.stats_new, 1)
            v.wait_ge(G.stats_new, NC)
            for n, kind in enumerate(stages):
                {"f0": f0_dve, "f1": f1_dve, "a0": att_dve, "a1": att_dve}[kind](n)


STAGES = ("f0", "a0", "f0", "f1", "a1", "f1")


def layout(inputs):
    i = {k: np.asarray(v) for k, v in inputs.items()}
    f = np.float32

    def rows(x, n=P):
        out = np.zeros((n, x.shape[1]), f)
        out[:x.shape[0]] = x
        return out

    gu, dn = i["L0_ffn_experts_gate_up"], i["L0_ffn_experts_down"]
    wg = rows(np.concatenate([gu[:, :I0].reshape(-1, H), i["L0_ffn_shared_gate_w"]]), MT0 * P).T
    wu = rows(np.concatenate([gu[:, I0:].reshape(-1, H), i["L0_ffn_shared_up_w"]]), MT0 * P).T
    wd = rows(np.concatenate([dn.transpose(0, 2, 1).reshape(-1, H), i["L0_ffn_shared_down_w"].T]), MT0 * P)
    wd = wd.reshape(MT0, P, H).transpose(1, 0, 2).reshape(P, MT0 * H)
    w0 = np.concatenate([wg, wu, wd], axis=1)
    sel = np.zeros((P, MT0 * P), f)
    for r in range(E0 * I0 + SI0):
        e = min(r // I0, E0)
        sel[e, r] = sel[32 + e, r] = 1

    s = {n: np.zeros((P, k), f) for n, k in SMALL.items()}
    wq, bq, wk, bk = (i[f"L0_attn_{n}"] for n in ("Wq", "bq", "Wk", "bk"))
    for g in range(NKV0):
        for c in range(3):
            at = 32 * g + HD0 * c
            s["wks"][:, at:at + HD0] = wk[:, g * HD0:(g + 1) * HD0]
            s["bqk"][at:at + HD0, GQ0] = bk[g * HD0:(g + 1) * HD0]
            for j in range(GQ0):
                h = g * GQ0 + j
                s["wqs"][:, j * P + at:j * P + at + HD0] = wq[:, h * HD0:(h + 1) * HD0]
                s["bqk"][at:at + HD0, j] = bq[h * HD0:(h + 1) * HD0]
        s["bqk"][32 * g + 24:32 * g + 26, GQ0] = -1
        s["masks"][32 * g + 16:32 * g + 24, 0] = -1
        s["masks"][32 * g + 8:32 * g + 16, 1] = -1
        s["masks"][32 * g:32 * g + 32, 2 + g] = 1
    s["masks"][64:96, 6] = -1
    s["masks"][32:64, 7] = -1
    s["masks"][97, 7] = -1
    s["wv"][:] = i["L0_attn_Wv"]
    s["bvb"][:] = i["L0_attn_bv"]
    s["wo"][:] = i["L0_attn_Wo"].reshape(GQ0, NKV0, HD0, H).transpose(1, 0, 2, 3).reshape(P, H)
    s["bo"][:] = i["L0_attn_bo"]
    s["w1"][:] = i["L1_ffn_W1"]
    s["b1"][:RH1, 0] = i["L1_ffn_b1"]
    s["w2"][:RH1] = i["L1_ffn_W2"]
    s["b2"][:] = i["L1_ffn_b2"]
    s["diag"][:NB] = np.eye(NB)
    s["rev"][:] = np.arange(E1, 0, -1)
    wdq, bdq = i["L1_attn_W_DQ"], i["L1_attn_b_DQ"]
    for c in range(3):
        s["wdqs"][:, c * DC1:(c + 1) * DC1] = wdq
        s["b1q"][c * DC1:(c + 1) * DC1, 0] = bdq
    s["b1q"][96:98, 0] = 1
    s["wkap"][:, :DC1] = i["L1_attn_W_DKV"]
    s["wkap"][:, DC1:] = i["L1_attn_W_KR"]
    s["b1k"][:DC1, 0] = i["L1_attn_b_DKV"]
    s["b1k"][DC1:DC1 + DR1, 0] = i["L1_attn_b_KR"]
    s["wckv"][:] = i["L1_attn_W_DKV"]
    s["bckv"][:] = i["L1_attn_b_DKV"]
    s["bo1"][:] = i["L1_attn_b_O"]
    s["gw"][:, :E0] = i["L0_ffn_gate_w"].T
    s["gw"][:, E0] = i["L0_ffn_shared_expert_gate_w"][0]
    s["eps"][:] = EPS
    s["ident"][:] = np.eye(P)
    s["ones"][:] = 1
    small = np.concatenate([s[n] for n in SMALL], axis=1)

    r = {n: np.zeros((P, k), f) for n, k in RAW1_PARTS.items()}

    def heads(w, b, d):
        w = np.concatenate([w, b[None]]).reshape(DC1 + 1, NH1, d)
        return w.transpose(2, 1, 0)

    uk = heads(i["L1_attn_W_UK"], i["L1_attn_b_UK"], DK1)
    uq = heads(i["L1_attn_W_UQ"], i["L1_attn_b_UQ"], DK1)
    qr = heads(i["L1_attn_W_QR"], i["L1_attn_b_QR"], DR1)
    uv = heads(i["L1_attn_W_UV"], i["L1_attn_b_UV"], DK1)
    wo = i["L1_attn_W_O"].reshape(NH1, DK1, H)
    for h in range(NH1):
        r["ukt"][:, h * KAP:h * KAP + DC1] = uk[:, h, :DC1]
        r["ukt"][:, h * KAP + KAP - 1] = uk[:, h, DC1]
        for c in range(3):
            r["uqt"][:, h * P + c * DC1:h * P + (c + 1) * DC1] = uq[:, h, :DC1]
        r["uqt"][:, h * P + 96] = r["uqt"][:, h * P + 97] = uq[:, h, DC1]
        r["qrp"][:DC1 + 1, h * KAP + DC1:h * KAP + DC1 + DR1] = qr[:, h, :].T
        at = h * P + 32 * (h % 4)
        r["uvt"][:, at:at + DC1] = uv[:, h, :DC1]
        r["wo"][:, h * H:(h + 1) * H] = wo[h]
        r["buv"][:, h] = uv[:, h, DC1]
        r["neg"][h, h * P:(h + 1) * P] = r["neg"][8 + h, h * P:(h + 1) * P] = -1
    for c in range(3):
        r["spread"][:DC1, c * DC1:(c + 1) * DC1] = np.eye(DC1)
    r["spread"][DC1, 96:98] = 1
    w1 = np.concatenate([r[n] for n in RAW1_PARTS], axis=1)

    zd = i["L1_ffn_Wb"].reshape(E1, FT1, P, H).transpose(0, 2, 1, 3).reshape(E1, P, FT1 * H)
    got = dict(x=i["L0_attn_x"], small=small, w0=w0, sel=sel, w1=w1, zone_up=i["L1_ffn_Wa"], zone_down=zd)
    return {k: np.ascontiguousarray(v) for k, v in got.items()}


def kernel(**inputs):
    import concourse.bacc as bacc
    from concourse.bass_utils import run_bass_kernel_spmd

    arrays = layout(inputs)
    nc = bacc.Bacc("TRN2", target_bir_lowering=False, num_devices=1)
    aps = {k: nc.dram_tensor(f"in_{k}", v.shape, F32, kind="ExternalInput").ap() for k, v in arrays.items()}
    out = nc.dram_tensor("out_x", arrays["x"].shape, F32, kind="ExternalOutput").ap()
    program(nc, names(aps), out, STAGES)
    r = run_bass_kernel_spmd(nc, [{f"in_{k}": v for k, v in arrays.items()}], core_ids=[0])
    return r.results[0]["out_x"]
```
